# Optimizing a Trainium2 kernel written in Bass

```python
import numpy as np
import jax
import jax.numpy as jnp

def _softmax(x, axis=-1):
    return jax.nn.softmax(x, axis=axis)

def _gelu(x):
    return jax.nn.gelu(x, approximate=True)

def _silu(x):
    return jax.nn.silu(x)

def _sigmoid(x):
    return jax.nn.sigmoid(x)

def _layernorm(x, axis=-1, eps=1e-05):
    m = jnp.mean(x, axis=axis, keepdims=True)
    v = jnp.var(x, axis=axis, keepdims=True)
    return (x - m) / jnp.sqrt(v + eps)

def _scatter_add(tgt, idx, src, axis=0):
    return tgt.at[idx].add(src)

def _segment_sum(src, seg, n):
    return jax.ops.segment_sum(src, seg, n)
kernel_name = 'mk_audio_tower_d1_tok_audfeat256_r4_0c22b2'

def setup_inputs(seed: int=0):
    np.random.seed(seed)
    _w = jnp.asarray

    def _rec_inputs():
        import jax
        import jax.numpy as jnp
        _rk = jax.random.key(seed)
        x = -0.000520686 + 1.00062 * jax.random.normal(jax.random.fold_in(_rk, 1), (64, 750, 64), jnp.float32)
        return x
    x = _rec_inputs()

    def _L0_tok_setup():
        import jax, jax.numpy as jnp
        import numpy as np
        BATCH = 2
        SEQ = 1024
        D_MODEL = 64
        N_STATE = 64
        DT_RANK = 1
        NUM_LAYERS = 3

        def _ssm_layer(x, A_log, Dp, W_dbc, W_dt, b_dt):
            A = -jnp.exp(A_log)
            dbc = jnp.einsum('ble,ce->blc', x, W_dbc)
            delta, Bm, Cm = jnp.split(dbc, [DT_RANK, DT_RANK + N_STATE], axis=-1)
            delta = jax.nn.softplus(jnp.einsum('blr,er->ble', delta, W_dt) + b_dt)
            dA = jnp.exp(delta[..., None] * A)
            dBx = (delta * x)[..., None] * Bm[:, :, None, :]

            def combine(c1, c2):
                a1, h1 = c1
                a2, h2 = c2
                return (a1 * a2, h1 * a2 + h2)
            _, hs = jax.lax.associative_scan(combine, (dA, dBx), axis=1)
            y = jnp.einsum('blen,bln->ble', hs, Cm)
            return y + Dp * x
        key = jax.random.key(seed)
        kx, kw1, kw2 = jax.random.split(key, 3)
        x = jax.random.normal(kx, (BATCH, SEQ, D_MODEL), dtype=jnp.float32)
        A_log = jnp.broadcast_to(jnp.log(jnp.arange(1, N_STATE + 1, dtype=jnp.float32)), (NUM_LAYERS, D_MODEL, N_STATE)).copy()
        D = jnp.ones((NUM_LAYERS, D_MODEL), dtype=jnp.float32)
        W_dbc = 0.02 * jax.random.normal(kw1, (NUM_LAYERS, DT_RANK + 2 * N_STATE, D_MODEL), dtype=jnp.float32)
        W_dt = 0.02 * jax.random.normal(kw2, (NUM_LAYERS, D_MODEL, DT_RANK), dtype=jnp.float32)
        b_dt = jnp.zeros((NUM_LAYERS, D_MODEL), dtype=jnp.float32)
        return {'x': x, 'A_log': A_log, 'D': D, 'W_dbc': W_dbc, 'W_dt': W_dt, 'b_dt': b_dt}
    _L0_tok_all = _L0_tok_setup()
    _L0_tok_in = {k: v for k, v in _L0_tok_all.items() if k in ('A_log', 'D', 'W_dbc', 'W_dt', 'b_dt')}
    del _L0_tok_all

    def _L0_attn_setup():
        import math
        import jax, jax.numpy as jnp
        import numpy as np
        D_MODEL = 64
        N_HEADS = 4
        HEAD_DIM = D_MODEL // N_HEADS
        MAX_REL = 30

        def _rel_pos_encodings(t, d_model):
            n = 2 * MAX_REL + 1
            positions = jnp.arange(n, dtype=jnp.float32)[:, None]
            div_term = jnp.exp(jnp.arange(0, d_model, 2, dtype=jnp.float32) * (-math.log(10000.0) / d_model))
            ang = positions * div_term
            enc = jnp.stack([jnp.sin(ang), jnp.cos(ang)], axis=-1).reshape(n, d_model)
            rng = jnp.arange(t)
            final_mat = jnp.clip(rng[None, :] - rng[:, None], -MAX_REL, MAX_REL) + MAX_REL
            return enc[final_mat]
        key = jax.random.key(seed)
        ks = jax.random.split(key, 12)
        d = D_MODEL
        s = 1.0 / math.sqrt(d)
        inp = {'inputs': jax.random.normal(ks[0], (16, 128, d), dtype=jnp.float32), 'ln_gamma': jnp.ones((d,), jnp.float32), 'ln_beta': jnp.zeros((d,), jnp.float32), 'Wq': jax.random.normal(ks[1], (d, d), jnp.float32) * s, 'bq': jnp.zeros((d,), jnp.float32), 'Wk': jax.random.normal(ks[2], (d, d), jnp.float32) * s, 'bk': jnp.zeros((d,), jnp.float32), 'Wv': jax.random.normal(ks[3], (d, d), jnp.float32) * s, 'bv': jnp.zeros((d,), jnp.float32), 'Wpos': jax.random.normal(ks[4], (d, d), jnp.float32) * s, 'bpos': jnp.zeros((d,), jnp.float32), 'Wo': jax.random.normal(ks[5], (d, d), jnp.float32) * s, 'bo': jnp.zeros((d,), jnp.float32), 'u_bias': jax.random.normal(ks[6], (1, N_HEADS, 1, HEAD_DIM), jnp.float32) * 0.02, 'v_bias': jax.random.normal(ks[7], (1, N_HEADS, 1, HEAD_DIM), jnp.float32) * 0.02}
        return inp
    _L0_attn_all = _L0_attn_setup()
    _L0_attn_in = {k: v for k, v in _L0_attn_all.items() if k in ('ln_gamma', 'ln_beta', 'Wq', 'bq', 'Wk', 'bk', 'Wv', 'bv', 'Wpos', 'bpos', 'Wo', 'bo', 'u_bias', 'v_bias')}
    del _L0_attn_all

    def _L0_ffn_setup():
        import jax, jax.numpy as jnp
        import numpy as np
        B, S, H, F, E, K = (8, 1024, 64, 128, 16, 2)
        EPS = 1e-05
        key = jax.random.key(seed)
        ks = jax.random.split(key, 9)
        sc = 0.02
        return {'x': jax.random.normal(ks[0], (B, S, H), dtype=jnp.float32), 'gate_w': jax.random.normal(ks[1], (H, E), dtype=jnp.float32) * sc, 'gate_b': jnp.zeros((E,), dtype=jnp.float32), 'w1': jax.random.normal(ks[2], (E, H, F), dtype=jnp.float32) * sc, 'b1': jnp.zeros((E, F), dtype=jnp.float32), 'w2': jax.random.normal(ks[3], (E, F, H), dtype=jnp.float32) * sc, 'b2': jnp.zeros((E, H), dtype=jnp.float32), 'gamma': jnp.ones((H,), dtype=jnp.float32), 'beta': jnp.zeros((H,), dtype=jnp.float32)}
    _L0_ffn_all = _L0_ffn_setup()
    _L0_ffn_in = {k: v for k, v in _L0_ffn_all.items() if k in ('gate_w', 'gate_b', 'w1', 'b1', 'w2', 'b2', 'gamma', 'beta')}
    del _L0_ffn_all
    return {'x': x, 'L0_tok_A_log': _L0_tok_in['A_log'], 'L0_tok_D': _L0_tok_in['D'], 'L0_tok_W_dbc': _L0_tok_in['W_dbc'], 'L0_tok_W_dt': _L0_tok_in['W_dt'], 'L0_tok_b_dt': _L0_tok_in['b_dt'], 'L0_attn_ln_gamma': _L0_attn_in['ln_gamma'], 'L0_attn_ln_beta': _L0_attn_in['ln_beta'], 'L0_attn_Wq': _L0_attn_in['Wq'], 'L0_attn_bq': _L0_attn_in['bq'], 'L0_attn_Wk': _L0_attn_in['Wk'], 'L0_attn_bk': _L0_attn_in['bk'], 'L0_attn_Wv': _L0_attn_in['Wv'], 'L0_attn_bv': _L0_attn_in['bv'], 'L0_attn_Wpos': _L0_attn_in['Wpos'], 'L0_attn_bpos': _L0_attn_in['bpos'], 'L0_attn_Wo': _L0_attn_in['Wo'], 'L0_attn_bo': _L0_attn_in['bo'], 'L0_attn_u_bias': _L0_attn_in['u_bias'], 'L0_attn_v_bias': _L0_attn_in['v_bias'], 'L0_ffn_gate_w': _L0_ffn_in['gate_w'], 'L0_ffn_gate_b': _L0_ffn_in['gate_b'], 'L0_ffn_w1': _L0_ffn_in['w1'], 'L0_ffn_b1': _L0_ffn_in['b1'], 'L0_ffn_w2': _L0_ffn_in['w2'], 'L0_ffn_b2': _L0_ffn_in['b2'], 'L0_ffn_gamma': _L0_ffn_in['gamma'], 'L0_ffn_beta': _L0_ffn_in['beta']}

def reference(x, L0_tok_A_log, L0_tok_D, L0_tok_W_dbc, L0_tok_W_dt, L0_tok_b_dt, L0_attn_ln_gamma, L0_attn_ln_beta, L0_attn_Wq, L0_attn_bq, L0_attn_Wk, L0_attn_bk, L0_attn_Wv, L0_attn_bv, L0_attn_Wpos, L0_attn_bpos, L0_attn_Wo, L0_attn_bo, L0_attn_u_bias, L0_attn_v_bias, L0_ffn_gate_w, L0_ffn_gate_b, L0_ffn_w1, L0_ffn_b1, L0_ffn_w2, L0_ffn_b2, L0_ffn_gamma, L0_ffn_beta):
    import jax
    import jax.numpy as jnp

    def _L0_tok_ref(x, A_log, D, W_dbc, W_dt, b_dt):
        import jax, jax.numpy as jnp
        import numpy as np
        BATCH = 2
        SEQ = 1024
        D_MODEL = 64
        N_STATE = 64
        DT_RANK = 1
        NUM_LAYERS = 3

        def _ssm_layer(x, A_log, Dp, W_dbc, W_dt, b_dt):
            A = -jnp.exp(A_log)
            dbc = jnp.einsum('ble,ce->blc', x, W_dbc)
            delta, Bm, Cm = jnp.split(dbc, [DT_RANK, DT_RANK + N_STATE], axis=-1)
            delta = jax.nn.softplus(jnp.einsum('blr,er->ble', delta, W_dt) + b_dt)
            dA = jnp.exp(delta[..., None] * A)
            dBx = (delta * x)[..., None] * Bm[:, :, None, :]

            def combine(c1, c2):
                a1, h1 = c1
                a2, h2 = c2
                return (a1 * a2, h1 * a2 + h2)
            _, hs = jax.lax.associative_scan(combine, (dA, dBx), axis=1)
            y = jnp.einsum('blen,bln->ble', hs, Cm)
            return y + Dp * x
        for i in range(NUM_LAYERS):
            x = _ssm_layer(x, A_log[i], D[i], W_dbc[i], W_dt[i], b_dt[i])
            if i < NUM_LAYERS - 1:
                b, l, d = x.shape
                x = x[:, :l // 2 * 2].reshape(b, l // 2, 2, d).mean(axis=2)
        return x

    def _L0_attn_ref(inputs, ln_gamma, ln_beta, Wq, bq, Wk, bk, Wv, bv, Wpos, bpos, Wo, bo, u_bias, v_bias):
        import math
        import jax, jax.numpy as jnp
        import numpy as np
        D_MODEL = 64
        N_HEADS = 4
        HEAD_DIM = D_MODEL // N_HEADS
        MAX_REL = 30

        def _rel_pos_encodings(t, d_model):
            n = 2 * MAX_REL + 1
            positions = jnp.arange(n, dtype=jnp.float32)[:, None]
            div_term = jnp.exp(jnp.arange(0, d_model, 2, dtype=jnp.float32) * (-math.log(10000.0) / d_model))
            ang = positions * div_term
            enc = jnp.stack([jnp.sin(ang), jnp.cos(ang)], axis=-1).reshape(n, d_model)
            rng = jnp.arange(t)
            final_mat = jnp.clip(rng[None, :] - rng[:, None], -MAX_REL, MAX_REL) + MAX_REL
            return enc[final_mat]
        b, t, d = inputs.shape
        h, hd = (N_HEADS, HEAD_DIM)
        mu = jnp.mean(inputs, axis=-1, keepdims=True)
        var = jnp.mean(jnp.square(inputs - mu), axis=-1, keepdims=True)
        x = (inputs - mu) * jax.lax.rsqrt(var + 1e-05) * ln_gamma + ln_beta

        def split_heads(y):
            return y.reshape(b, t, h, hd).transpose(0, 2, 1, 3)
        q = split_heads(x @ Wq.T + bq)
        k = split_heads(x @ Wk.T + bk)
        v = split_heads(x @ Wv.T + bv)
        rel = jax.lax.stop_gradient(_rel_pos_encodings(t, d))
        pos = (rel @ Wpos.T + bpos).reshape(t, t, h, hd)
        qk_score = jnp.einsum('bhtd,bhsd->bhts', q + u_bias, k)
        pos_score = jnp.einsum('bhtd,tshd->bhts', q + v_bias, pos)
        scores = (qk_score + pos_score) / math.sqrt(hd)
        attn = jax.nn.softmax(scores, axis=-1)
        ctx = jnp.einsum('bhts,bhsd->bhtd', attn, v)
        ctx = ctx.transpose(0, 2, 1, 3).reshape(b, t, d)
        return ctx @ Wo.T + bo

    def _L0_ffn_ref(x, gate_w, gate_b, w1, b1, w2, b2, gamma, beta):
        import jax, jax.numpy as jnp
        import numpy as np
        B, S, H, F, E, K = (8, 1024, 64, 128, 16, 2)
        EPS = 1e-05
        gate_logits = x @ gate_w + gate_b
        topk_vals, topk_idx = jax.lax.top_k(gate_logits, K)
        topk_w = jax.nn.softmax(topk_vals, axis=-1)
        h = jax.nn.relu(jnp.einsum('bsh,ehf->bsef', x, w1) + b1)
        expert_out = jnp.einsum('bsef,efh->bseh', h, w2) + b2
        sel = jnp.take_along_axis(expert_out, topk_idx[:, :, :, None], axis=2)
        moe = jnp.sum(topk_w[..., None] * sel, axis=2)
        y = x + moe
        mu = jnp.mean(y, axis=-1, keepdims=True)
        var = jnp.var(y, axis=-1, keepdims=True)
        return (y - mu) / jnp.sqrt(var + EPS) * gamma + beta
    h = _L0_tok_ref(x, L0_tok_A_log, L0_tok_D, L0_tok_W_dbc, L0_tok_W_dt, L0_tok_b_dt)
    h = h + _L0_attn_ref(_layernorm(h, axis=-1), L0_attn_ln_gamma, L0_attn_ln_beta, L0_attn_Wq, L0_attn_bq, L0_attn_Wk, L0_attn_bk, L0_attn_Wv, L0_attn_bv, L0_attn_Wpos, L0_attn_bpos, L0_attn_Wo, L0_attn_bo, L0_attn_u_bias, L0_attn_v_bias)
    h = h + _L0_ffn_ref(_layernorm(h, axis=-1), L0_ffn_gate_w, L0_ffn_gate_b, L0_ffn_w1, L0_ffn_b1, L0_ffn_w2, L0_ffn_b2, L0_ffn_gamma, L0_ffn_beta)
    return h

_drawn_inputs = setup_inputs


def setup_inputs(seed=0):
    import zlib

    import numpy as np

    out = dict(_drawn_inputs(seed))
    spreads = {'L0_tok_D': (1.0, 0.2),
     'L0_tok_b_dt': (0.0, 0.634),
     'L0_attn_ln_gamma': (1.0, 0.2),
     'L0_attn_ln_beta': (0.0, 0.1),
     'L0_attn_bq': (0.0, 0.1),
     'L0_attn_bk': (0.0, 2.0),
     'L0_attn_bv': (0.0, 0.1),
     'L0_attn_bpos': (0.0, 2.0),
     'L0_attn_bo': (0.0, 0.1),
     'L0_ffn_gate_b': (0.0, 0.1),
     'L0_ffn_b1': (0.0, 0.8),
     'L0_ffn_b2': (0.0, 0.1),
     'L0_ffn_gamma': (1.0, 0.2),
     'L0_ffn_beta': (0.0, 0.1)}
    factors = {'L0_tok_A_log': 5.765,
     'L0_tok_W_dt': 22.879,
     'L0_attn_u_bias': 6.902,
     'L0_attn_v_bias': 8.0,
     'L0_ffn_w1': 5.938,
     'L0_ffn_w2': 4.514}
    for name, (base, spread) in spreads.items():
        noise = np.random.default_rng([zlib.crc32(name.encode()), seed]).standard_normal(out[name].shape)
        drawn = base * np.exp(spread * noise) if base else spread * noise
        out[name] = jnp.asarray(drawn.astype(out[name].dtype))
    for name, factor in factors.items():
        out[name] = (out[name] * factor).astype(out[name].dtype)
    return out
```

```python
from contextlib import ExitStack

import numpy as np

import concourse.bass as bass
from concourse import mybir

ALU = mybir.AluOpType
ACT = mybir.ActivationFunctionType
F32 = mybir.dt.float32
BF16 = mybir.dt.bfloat16

E = 64
BATCH = 64
PAIRS = BATCH // 2
LENGTHS = (750, 375, 187)
LAYERS = len(LENGTHS)
GROUPS = 4
GE = E // GROUPS
CH = 16
SEG = 4 * CH
SEGS = tuple(-(-n // SEG) for n in LENGTHS)
PADDED = tuple(s * SEG for s in SEGS)
EPS = (1, 2, 4)
STEPS = tuple(E // e for e in EPS)
SPG = tuple(s // GROUPS for s in STEPS)
BANKS = tuple(-(-s // 2) for s in SEGS)
SETS = tuple(-(-b // 3) for b in BANKS)
BX_RING = 4
LEAD = 1
MEAN = 3
HALVES = (((0, 384), (384, 750)), ((0, 375),), ((0, 187),))
WIDE = (((0, 384), (384, 768)), ((0, 384),), ((0, 192),))
TURN = 125
TURNS = LENGTHS[0] // TURN


def feature_columns(k):
    n = LENGTHS[k]
    return ((0,), (0, 512), (0, n, 512, 512 + n))[k]


def chain(k):
    s = [("turn", 0), ("turned", 0), ("turn", 1), ("turned", 1)] if k == 0 else [("mean", c) for c in range(0, SEGS[k - 1], MEAN)] + [("mixed", 0)]
    halves = range(len(HALVES[k]))
    for h in halves:
        s += [("z", h), ("zout", h)]
    s += [("exp", 0), ("round", 0), ("log", 0), ("slip", 0), ("fix", 0), ("delta", 0), ("u", 0),
          ("high", 0), ("rest", 0), ("middle", 0), ("low", 0), ("stack", 0)]
    for h in halves:
        s += [("b", h), ("bout", h)]
    for h in halves:
        s += [("c", h), ("cout", h)]
    return s


BY_DMA = ("stack", "laststore")
CHAINS = {0: chain(0), 1: chain(1), 2: chain(2), "keep1": [("keep", 0)], "keep2": [("keep", 0)],
          "last": [("last", 0), ("lastout", 0), ("laststore", 0)]}
DELAY = {"turn": 2, "mean": 1, "z": 2, "b": 2, "c": 2, "last": 2, "log": 1, "high": 2, "middle": 2}
START = (10, 1, 0)
ORDER = (("keep2", 2), (1, 1), ("last", 3), (2, 2), ("keep1", 0), (0, -1))
ITERATIONS = PAIRS + 3
FIRST_FULL, LAST_FULL = 4, PAIRS - 1


def partition_of(place):
    group, row = divmod(place, GE)
    return GROUPS * row + group


def feature_order(k):
    order = list(range(E))
    for _ in range(k):
        order = [order[partition_of(p)] for p in range(E)]
    return order


assert feature_order(LAYERS) == list(range(E))


def clamp(m):
    return min(max(m, 0), PAIRS)


def linear(i, parts):
    if isinstance(i, int):
        return sum(w * clamp(i + d) for w, d in parts)
    return i * sum(w for w, _ in parts) + sum(w * d for w, d in parts)


def before(i, stage, weights):
    return linear(i, [(weights[0], int(stage > 0)), (weights[1], -1 + int(stage > 1)), (weights[2], -2)])


def chain_before(i, kind):
    parts, reached = [], False
    for name, lag in ORDER:
        reached = reached or name == kind
        parts.append((counted(name), -lag + int(not reached)))
    return linear(i, parts)


def counted(kind):
    return sum(name not in BY_DMA for name, _ in CHAINS[kind])


def chained(i, kind, step):
    steps = [s for s in CHAINS[kind] if s[0] not in BY_DMA]
    return chain_before(i, kind) + steps.index(step) + 1


def stacks_before(i, kind):
    parts, reached = [], False
    for name, lag in ORDER:
        reached = reached or name == kind
        if name in (0, 1, 2):
            parts.append((1, -lag + int(not reached)))
    return linear(i, parts)


def runs(i, kind):
    lag = dict(ORDER)[kind]
    return not isinstance(i, int) or 0 <= i - lag < PAIRS


def has(i, stage):
    return not isinstance(i, int) or 0 <= i - stage < PAIRS


def stage_before(i, stage):
    while True:
        i, stage = (i, stage - 1) if stage else (i - 1, LAYERS - 1)
        if has(i, stage):
            return i, stage
        if i < 0:
            return None


def due(value):
    return not isinstance(value, int) or value > 0


def fixed(eng, value):
    return value if isinstance(value, int) else eng.to_reg(value)


def segment_jobs(stage, slot):
    q = slot - SPG[stage] - 1
    g, c = divmod(q, SPG[stage])
    if g >= GROUPS - 1 and stage < LAYERS - 1:
        q -= (GROUPS - 1) * SPG[stage]
        return [(GROUPS - 1, c) for c in (2 * q, 2 * q + 1) if c < SEGS[stage]]
    return [(g, c)] if q >= 0 and g < GROUPS and c < SEGS[stage] else []


def iteration_plan(i):
    ahead = {0: [], 1: [], 2: []}
    for kind in ("keep2", 1, "last", 2):
        if runs(i, kind):
            ahead[0] += [(kind, s) for s in CHAINS[kind]]
    for kind in ("keep1", 0):
        if runs(i, kind):
            ahead[1] += [(kind, s) for s in CHAINS[kind]]
    mains = [(stage, 0, s) for stage in range(LAYERS) if has(i, stage) for s in range(STEPS[stage])]
    ahead_of_time = [(0, -1, s) for s in range(LEAD)] if has(i + 1, 0) else []
    begun = min(LEAD, len(mains)) if has(i, 0) and not (isinstance(i, int) and i == 0) else 0
    to_feed = mains[begun:]
    if has(i, LAYERS - 1):
        to_feed, ahead_of_time = to_feed + ahead_of_time, []
    fed = begun
    step = 0
    plan = []
    for stage in range(LAYERS):
        prior, lag = ((2, 1), (0, 0), (1, 0))[stage]
        spilled = has(i - lag, prior)
        todo = list(ahead[stage])
        for slot in range(STEPS[stage]):
            if has(i, stage):
                while fed <= step + LEAD and to_feed:
                    plan.append(("feed",) + to_feed.pop(0))
                    fed += 1
                plan.append(("main", stage, slot))
                step += 1
                for g, c in segment_jobs(stage, slot):
                    plan.append(("seg", stage, 0, g, c))
            if spilled:
                for g, c in segment_jobs(prior, STEPS[prior] + slot):
                    plan.append(("seg", prior, lag, g, c))
            if todo and slot == START[stage]:
                due = slot
            while todo and slot >= START[stage] and slot >= due:
                plan.append(("chain",) + todo.pop(0))
                due += DELAY.get(todo[0][1][0], 0) if todo else 0
        assert not todo
    plan += [("feed",) + f for f in to_feed + ahead_of_time]
    return plan


def state_space_layers(nc, ctx, x, weights, scratch, hidden):
    def sb(name, shape, dt=F32):
        return ctx.enter_context(nc.sbuf_tensor(name, shape, dt))

    def ps(name, shape):
        return ctx.enter_context(nc.psum_tensor(name, shape, F32))

    def sem(name):
        return ctx.enter_context(nc.semaphore(name))

    pick = sb("pick", [96, GE, 128], BF16)
    ident = sb("ident", [128, 128])
    halver = sb("halver", [SEG, SEG // 2])
    w_state = sb("w_state", [128, LAYERS, 2, 128])
    w_delta = sb("w_delta", [128, LAYERS, 128])
    rank_in = sb("rank_in", [128, LAYERS])
    b_dt = sb("b_dt", [128, LAYERS])
    d_skip = sb("d_skip", [128, LAYERS])
    skip = sb("skip", [128, LAYERS, 128])
    decay = sb("decay", [128, LAYERS, E])
    xT = [sb(f"xT{k}", [128, PADDED[k]]) for k in range(LAYERS)]
    kept = [None] + [sb(f"kept{k}", [128, LENGTHS[k]]) for k in (1, 2)]
    stack = [sb(f"stack{k}", [96, 2, GROUPS, LENGTHS[k]], BF16) for k in range(LAYERS)]
    b_in = [sb(f"b_in{k}", [128, LENGTHS[k]]) for k in range(LAYERS)]
    c_out = [sb(f"c_out{k}", [128, PADDED[k] // CH, 2, CH]) for k in range(LAYERS)]
    n0 = LENGTHS[0]
    t_decay = sb("t_decay", [128, n0])
    t_delta = sb("t_delta", [128, TURNS * 128])
    part = sb("part", [128, 2, 3, n0], BF16)
    early = part[:, :, :, :].rearrange("p v q l -> p (v q l)").bitcast(F32)
    t_relu, t_slip = early[:, 0:n0], early[:, n0:2 * n0]
    x_nat = t_delta[0:TURN, :].rearrange("p (c b e) -> p c b e", b=2, e=E)
    u_wide = sb("u_wide", [128, 2, n0])
    b_x = sb("b_x", [128, BX_RING, n0])
    h = sb("h", [128, 2, GE * PADDED[0]])
    y_sb = sb("y_sb", [128, 2, 6, CH, GE])
    y_nat = [sb(f"y_nat{k}", [SEG, SEGS[k], 2, E]) for k in range(LAYERS)]
    h_out = sb("h_out", [SEG, 3, 128])

    ps_d = ps("ps_d", [128, 2, 1024])
    ps_u = ps("ps_u", [128, 1024])
    ps_y = ps("ps_y", [128, 512])
    ps_r = ps("ps_r", [128, 512])

    consts_in = sem("consts_in")
    setup_act = sem("setup_act")
    setup_dve = sem("setup_dve")
    cleared = sem("cleared")
    d_ready = sem("d_ready")
    u_ready = sem("u_ready")
    decay_ready = sem("decay_ready")
    u_copied = sem("u_copied")
    bx_made = sem("bx_made")
    scanned = sem("scanned")
    y_ready = sem("y_ready")
    y_copied = sem("y_copied")
    stored = [[sem(f"stored{k}_{n}") for n in range(2)] for k in range(LAYERS)]
    y_loaded = [[sem(f"y_loaded{k}_{g}") for g in range(2)] for k in range(LAYERS)]
    x_loaded = sem("x_loaded")
    stacked = sem("stacked")
    chain_done = sem("chain_done")
    h_stored = sem("h_stored")

    STACK_DMAS = 12
    LOAD = 8 * 16
    all_banks = tuple(GROUPS * b for b in BANKS)

    def bank_count(i, stage, g, bank):
        return before(i, stage, all_banks) + g * BANKS[stage] + bank

    def store_count(i, stage, n):
        per = GROUPS * SETS[stage] // 2
        return linear(i, [(16 * per, -stage)]) + 16 * (n // 2 + 1)

    def load_count(i, stage, g):
        return linear(i, [(LOAD * GROUPS // 2, -stage)]) + LOAD * (g // 2 + 1)

    def operands_count(i, stage):
        return chain_before(i, "keep2" if stage == 0 else "keep1")

    def everywhere(eng, iteration):
        for i in range(FIRST_FULL):
            iteration(i)
        with eng.Fori(FIRST_FULL, LAST_FULL) as i:
            iteration(i)
        for i in range(LAST_FULL, ITERATIONS + 1):
            iteration(i)

    block = ctx.enter_context(nc.Block())

    @block.sync
    def _(sp):
        for dst, src in ((pick[:, :, :], weights["pick"]), (ident[:, :], weights["ident"]),
                         (halver[:, :], weights["halver"]), (w_state[:, :, :, :], weights["w_state"]),
                         (w_delta[:, :, :], weights["w_dt"]), (rank_in[:, :], weights["rank_in"]),
                         (b_dt[:, :], weights["b_dt"]), (d_skip[:, :], weights["d_skip"]),
                         (decay[:, :, :], weights["a_log"]), (skip[:, :, :], weights["skip"])):
            sp.dma_start(dst, src).then_inc(consts_in, 16)

        def load_x(pair, users=0):
            frm = [x[pair, b] for b in range(2)]
            if due(users):
                sp.wait_ge(chain_done, users)
            for b in range(2):
                sp.dma_start(x_nat[:, :, b, :], frm[b]).then_inc(x_loaded, 16)

        load_x(0)

        def stack_operands(i, kind):
            parts = fixed(sp, chained(i, kind, ("low", 0)))
            used = fixed(sp, before(i, 1 if kind == 0 else 0, STEPS))
            sp.wait_ge(chain_done, parts)
            if due(used):
                sp.wait_ge(u_ready, used)
            n = LENGTHS[kind]
            for v in range(2):
                for p in range(3):
                    for b in range(2):
                        row = 32 * p + 16 * b
                        sp.dma_start(stack[kind][row:row + 16, v, :, :],
                                     part[64 * b:64 * b + 64, v, p, 0:n])\
                          .then_inc(stacked, 16)

        def store_set(i, stage, g, w):
            s0, s1 = 6 * w, min(6 * w + 6, SEGS[stage])
            n = g * SETS[stage] + w
            last_bank = min(3 * w + 3, BANKS[stage]) - 1
            copied = fixed(sp, bank_count(i, stage, g, last_bank) + 1)
            reread = fixed(sp, load_count(i, stage, g - 2))
            sp.wait_ge(y_copied, copied)
            if w == 0 and due(reread):
                sp.wait_ge(y_loaded[stage][g % 2], reread)
            sp.dma_start(scratch[stage][g % 2, :, s0:s1, :, :], y_sb[:, n % 2, 0:s1 - s0, :, :])\
              .then_inc(stored[stage][n % 2], 16)

        def load_y(i, stage, g):
            sets = [(g * SETS[stage] + w) for w in range(SETS[stage])]
            in_dram = [fixed(sp, store_count(i, stage, n)) for n in sets]
            used = fixed(sp, chain_before(i, "last" if stage == 0 else "keep1"))
            for n, count in zip(sets, in_dram):
                sp.wait_ge(stored[stage][n % 2], count)
            if g == 0:
                sp.wait_ge(chain_done, used)
            row = SEGS[stage] * CH * GE
            frm = scratch[stage][g % 2].rearrange("p c l e -> (p c l e)")
            for t in range(4):
                for b in range(2):
                    first = (32 * t + 16 * b) * row
                    diagonal = bass.AP(tensor=frm.tensor, offset=frm.offset + first,
                                       ap=[[row + GE, CH], [CH * GE, SEGS[stage]], [1, GE]])
                    sp.dma_start(y_nat[stage][CH * t:CH * t + CH, :, b, g * GE:(g + 1) * GE], diagonal)\
                      .then_inc(y_loaded[stage][g % 2], 16)

        def store_hidden(i):
            full = LENGTHS[2] // SEG
            tail = LENGTHS[2] - full * SEG
            to = hidden[i - 3]
            parts = [(to[b, 0:full * SEG, :].rearrange("(c q) e -> q c e", q=SEG), to[b, full * SEG:, :])
                     for b in range(2)]
            sp.wait_ge(chain_done, chained(i, "last", ("lastout", 0)))
            for b, (head, rest) in enumerate(parts):
                sp.dma_start(head, h_out[:, 0:full, 64 * b:64 * b + 64]).then_inc(h_stored, 16)
                sp.dma_start(rest, h_out[0:tail, full, 64 * b:64 * b + 64]).then_inc(h_stored, 16)

        stack_operands(-1, 0)

        def iteration(i):
            for what in iteration_plan(i):
                if what[0] == "seg":
                    _, stage, lag, g, c = what
                    if c % 6 == 5 or c == SEGS[stage] - 1:
                        store_set(i - lag, stage, g, c // 6)
                        if c == SEGS[stage] - 1:
                            load_y(i - lag, stage, g)
                elif what[0] == "chain" and what[2][0] == "stack":
                    stack_operands(i, what[1])
                elif what[0] == "chain" and what[2][0] == "laststore":
                    store_hidden(i)
                if what == ("chain", "keep1", ("keep", 0)) and runs(i, 0):
                    load_x(i + 1, chain_before(i, "keep1"))

        everywhere(sp, iteration)
        sp.wait_ge(h_stored, 64 * PAIRS)

    @block.scalar
    def _(act):
        act.preload_act_table_set("natural_log_exp_and_others")
        act.wait_ge(consts_in, 16 * 10)
        act.activation(decay[:, :, :], decay[:, :, :], ACT.Exp).then_inc(setup_act, 1)
        act.wait_ge(setup_dve, 5)

        def chain_step(i, kind, step):
            name, half = step
            if name in BY_DMA or kind not in (0, 1, 2):
                return
            n = LENGTHS[kind]
            previous = chained(i, kind, step) - 1
            if name == "turned":
                act.wait_ge(chain_done, previous)
                cols = TURNS // 2
                to = xT[0][:, 0:n].rearrange("p (q c) -> p c q", c=TURNS)[:, half * cols:(half + 1) * cols, :]
                act.activation(to, ps_r[:, 0:cols * TURN].rearrange("p (c q) -> p c q", c=cols), ACT.Copy)\
                   .then_inc(chain_done, 1)
            elif name == "zout":
                act.wait_ge(chain_done, previous)
                if due(count := stacks_before(i, kind) * (16 * STACK_DMAS)):
                    act.wait_ge(stacked, count)
                a, b = HALVES[kind][half]
                act.activation(t_decay[:, a:b], ps_r[:, 0:b - a], ACT.Abs, bias=b_dt[:, kind:kind + 1])
                act.activation(t_relu[:, a:b], ps_r[:, 0:b - a], ACT.Relu, bias=b_dt[:, kind:kind + 1])\
                   .then_inc(chain_done, 1)
            elif name == "exp":
                act.wait_ge(chain_done, previous)
                act.activation(t_decay[:, 0:n], t_decay[:, 0:n], ACT.Exp, scale=-1.0).then_inc(chain_done, 1)
            elif name == "log":
                act.wait_ge(chain_done, previous)
                act.activation(t_delta[:, 0:n], t_decay[:, 0:n], ACT.Ln, bias=1.0).then_inc(chain_done, 1)
            elif name == "high":
                act.wait_ge(chain_done, previous)
                act.activation(part[:, 0, 0, 0:n], t_delta[:, 0:n], ACT.Copy)
                act.activation(part[:, 1, 0, 0:n], t_decay[:, 0:n], ACT.Copy).then_inc(chain_done, 1)
            elif name == "cout":
                act.wait_ge(chain_done, previous)
                if due(count := before(i, 1 if kind == 0 else 0, all_banks)):
                    act.wait_ge(y_ready, count)
                a, b = WIDE[kind][half]
                for s in range(2):
                    rows = slice(64 * s, 64 * s + 64)
                    last = act.activation(c_out[kind][rows, a // CH:b // CH, s, :],
                                          ps_r[rows, 0:b - a].rearrange("p (c l) -> p c l", l=CH), ACT.Copy)
                last.then_inc(chain_done, 1)

        for step in CHAINS[0]:
            chain_step(-1, 0, step)

        def decay_of_step(i, stage, s):
            act.wait_ge(d_ready, before(i, stage, STEPS) + s + 1)
            n = LENGTHS[stage]
            for j, col in enumerate(feature_columns(stage)):
                e = partition_of(s * EPS[stage] + j)
                d = ps_d[:, s % 2, col:col + n]
                last = act.activation(d, d, ACT.Exp, scale=decay[:, stage, e:e + 1])
            last.then_inc(decay_ready, 1)

        def copy_u(i, stage, s):
            act.wait_ge(u_ready, before(i, stage, STEPS) + s + 1)
            if due(count := before(i, stage, STEPS) + s - 1):
                act.wait_ge(bx_made, count)
            n = LENGTHS[stage]
            if stage == 0:
                last = act.activation(u_wide[:, s % 2, 0:n], ps_u[:, 0:n], ACT.Copy)
            else:
                half = EPS[stage] // 2 * n
                last = act.activation(u_wide[:, s % 2, 0:2 * half].rearrange("p (a f) -> p a f", a=2),
                                      ps_u[:, :].rearrange("p (a f) -> p a f", a=2)[:, :, 0:half], ACT.Copy)
            last.then_inc(u_copied, 1)

        def copy_y(i, stage, g, bank):
            n = g * SETS[stage] + bank // 3
            if bank % 3 == 0:
                prior = stage_before(i, stage)
                if n >= 2:
                    act.wait_ge(stored[stage][n % 2], store_count(i, stage, n - 2))
                elif prior is not None:
                    sets = GROUPS * SETS[prior[1]]
                    act.wait_ge(stored[prior[1]][n % 2], store_count(*prior, sets + n - 2))
            act.wait_ge(y_ready, bank_count(i, stage, g, bank) + 1)
            c0 = 2 * (bank % 3)
            segs = min(2, SEGS[stage] - 2 * bank)
            to = y_sb[:, n % 2, c0:c0 + segs, :, :].rearrange("p s l e -> p s e l")
            frm = ps_y[:, 0:256 * segs].rearrange("p (s e l) -> p s e l", e=GE, l=CH)
            act.activation(to, frm, ACT.Copy).then_inc(y_copied, 1)

        def iteration(i):
            for what in iteration_plan(i):
                if what[0] == "main":
                    decay_of_step(i, what[1], what[2])
                elif what[0] == "feed":
                    copy_u(i - what[2], what[1], what[3])
                elif what[0] == "seg":
                    _, stage, lag, g, c = what
                    if c % 2 == 1 or c == SEGS[stage] - 1:
                        copy_y(i - lag, stage, g, c // 2)
                else:
                    chain_step(i, what[1], what[2])

        everywhere(act, iteration)

    @block.vector
    def _(dve):
        for b in range(2):
            dve.memset(h[:, b, :], 0.0)
        for k in range(LAYERS):
            dve.memset(xT[k][:, LENGTHS[k]:], 0.0)
            dve.memset(c_out[k][:, :, :, :], 0.0).then_inc(cleared, 1)
        dve.wait_ge(consts_in, 16 * 10)
        for k in range(LAYERS):
            dve.tensor_scalar(w_delta[:, k, :], w_delta[:, k, :], rank_in[:, k:k + 1], None, ALU.mult)
        for k in range(LAYERS):
            last = dve.tensor_scalar(skip[:, k, :], skip[:, k, :], d_skip[:, k:k + 1], 0.5 if k < 2 else 1.0,
                                     ALU.mult, ALU.mult)
        last.then_inc(setup_dve, 4)
        dve.wait_ge(setup_act, 1)
        dve.tensor_scalar(decay[:, :, :], decay[:, :, :], -1.0, None, ALU.mult).then_inc(setup_dve, 1)

        def chain_step(i, kind, step):
            name = step[0]
            if name in BY_DMA:
                return
            n = LENGTHS[kind] if kind in (0, 1, 2) else 0
            previous = chained(i, kind, step) - 1
            if name == "mixed":
                dve.wait_ge(chain_done, previous)
                dve.tensor_copy(xT[kind][:, 0:n], ps_r[:, 0:n]).then_inc(chain_done, 1)
            elif name == "round":
                dve.wait_ge(chain_done, previous)
                dve.tensor_scalar(t_slip[:, 0:n], t_decay[:, 0:n], 1.0, -1.0, ALU.add, ALU.add)\
                   .then_inc(chain_done, 1)
            elif name == "slip":
                dve.wait_ge(chain_done, previous)
                dve.tensor_tensor(t_slip[:, 0:n], t_slip[:, 0:n], t_decay[:, 0:n], ALU.subtract)\
                   .then_inc(chain_done, 1)
            elif name == "fix":
                dve.wait_ge(chain_done, previous)
                dve.tensor_tensor(t_delta[:, 0:n], t_delta[:, 0:n], t_slip[:, 0:n], ALU.subtract)\
                   .then_inc(chain_done, 1)
            elif name == "bout":
                dve.wait_ge(chain_done, previous)
                if due(count := before(i, 1 if kind == 0 else 0, STEPS)):
                    dve.wait_ge(bx_made, count)
                a, b = HALVES[kind][step[1]]
                dve.tensor_copy(b_in[kind][:, a:b], ps_r[:, 0:b - a]).then_inc(chain_done, 1)
            elif name == "middle":
                dve.wait_ge(chain_done, previous)
                dve.tensor_copy(part[:, 0, 1, 0:n], t_delta[:, 0:n])
                dve.tensor_copy(part[:, 1, 1, 0:n], t_decay[:, 0:n]).then_inc(chain_done, 1)
            elif name == "rest":
                dve.wait_ge(chain_done, previous)
                dve.tensor_tensor(t_delta[:, 0:n], t_delta[:, 0:n], part[:, 0, 0, 0:n], ALU.subtract)
                dve.tensor_tensor(t_decay[:, 0:n], t_decay[:, 0:n], part[:, 1, 0, 0:n], ALU.subtract)\
                   .then_inc(chain_done, 1)
            elif name == "low":
                dve.wait_ge(chain_done, previous)
                dve.tensor_tensor(part[:, 0, 2, 0:n], t_delta[:, 0:n], part[:, 0, 1, 0:n], ALU.subtract)
                dve.tensor_tensor(part[:, 1, 2, 0:n], t_decay[:, 0:n], part[:, 1, 1, 0:n], ALU.subtract)\
                   .then_inc(chain_done, 1)
            elif name == "delta":
                dve.wait_ge(chain_done, previous)
                dve.tensor_tensor(t_delta[:, 0:n], t_delta[:, 0:n], t_relu[:, 0:n], ALU.add).then_inc(chain_done, 1)
            elif name == "u":
                dve.wait_ge(chain_done, previous)
                dve.tensor_tensor(t_decay[:, 0:n], t_delta[:, 0:n], xT[kind][:, 0:n], ALU.mult)\
                   .then_inc(chain_done, 1)
            elif name == "lastout":
                dve.wait_ge(chain_done, previous)
                if due(count := linear(i, [(64, -3)])):
                    dve.wait_ge(h_stored, count)
                full = LENGTHS[2] // SEG
                tail = LENGTHS[2] - full * SEG
                dve.tensor_copy(h_out[:, 0:full, :], ps_r[0:SEG, 0:128 * full].rearrange("p (c f) -> p c f", f=128))
                dve.tensor_copy(h_out[0:tail, full, :], ps_r[0:tail, 128 * full:128 * full + 128])\
                   .then_inc(chain_done, 1)

        for step in CHAINS[0]:
            chain_step(-1, 0, step)

        def recurrence(i, stage, s):
            n = LENGTHS[stage]
            done = before(i, stage, STEPS)
            g, place = divmod(s, SPG[stage])
            if place == 0:
                banks = before(i, stage, all_banks)
                if g == 0:
                    prior = stage_before(i, stage)
                    if prior is not None:
                        if due(count := banks - BANKS[prior[1]]):
                            dve.wait_ge(y_ready, count)
                else:
                    if due(count := banks + (g - 1) * BANKS[stage]):
                        dve.wait_ge(y_ready, count)
            dve.wait_ge(bx_made, done + s + 1)
            dve.wait_ge(decay_ready, done + s + 1)
            for j, col in enumerate(feature_columns(stage)):
                e = place * EPS[stage] + j
                to = h[:, g % 2, e * PADDED[stage]:e * PADDED[stage] + n]
                last = dve.tensor_tensor_scan(to, ps_d[:, s % 2, col:col + n], b_x[:, s % BX_RING, j * n:(j + 1) * n],
                                              0.0, ALU.mult, ALU.add)
            last.then_inc(scanned, 1)

        def iteration(i):
            for what in iteration_plan(i):
                if what[0] == "main":
                    recurrence(i, what[1], what[2])
                elif what[0] == "chain":
                    chain_step(i, what[1], what[2])

        everywhere(dve, iteration)

    @block.gpsimd
    def _(pool):
        def chain_step(i, kind, step):
            name = step[0]
            if name == "keep":
                pool.wait_ge(chain_done, chained(i, kind, step) - 1)
                k = int(kind[-1])
                n = LENGTHS[k]
                pairs = xT[k - 1][:, 0:2 * n].rearrange("p (l t) -> p l t", t=2)
                pool.tensor_tensor(kept[k][:, 0:n], pairs[:, :, 0], pairs[:, :, 1], ALU.add).then_inc(chain_done, 1)

        for step in CHAINS[0]:
            chain_step(-1, 0, step)

        def input_term(i, stage, s):
            n, f = LENGTHS[stage], EPS[stage]
            if s == 0:
                pool.wait_ge(chain_done, operands_count(i, stage))
            pool.wait_ge(u_copied, before(i, stage, STEPS) + s + 1)
            if due(count := before(i, stage, STEPS) + s - BX_RING + 1):
                pool.wait_ge(scanned, count)
            if f == 1:
                last = pool.tensor_tensor(b_x[:, s % BX_RING, 0:n], u_wide[:, s % 2, 0:n], b_in[0][:, 0:n], ALU.mult)
            else:
                last = pool.tensor_tensor(b_x[:, s % BX_RING, 0:f * n].rearrange("p (f l) -> p f l", f=f),
                                          u_wide[:, s % 2, 0:f * n].rearrange("p (f l) -> p f l", f=f),
                                          b_in[stage][:, None, 0:n].to_broadcast([128, f, n]), ALU.mult)
            last.then_inc(bx_made, 1)

        def iteration(i):
            for what in iteration_plan(i):
                if what[0] == "feed":
                    input_term(i - what[2], what[1], what[3])
                elif what[0] == "chain":
                    chain_step(i, what[1], what[2])

        everywhere(pool, iteration)

    @block.tensor
    def _(pe):
        pe.wait_ge(consts_in, 16 * 10)
        pe.wait_ge(cleared, LAYERS)

        def chain_step(i, kind, step):
            name, half = step
            if name == "turn":
                if due(count := chained(i, kind, step) - 1):
                    pe.wait_ge(chain_done, count)
                pe.wait_ge(x_loaded, linear(i, [(32, 1)]) + 32)
                for c in range(TURNS // 2):
                    t = half * (TURNS // 2) + c
                    last = pe.transpose(ps_r[:, c * TURN:(c + 1) * TURN],
                                        x_nat[:, t, :, :].rearrange("p b e -> p (b e)"),
                                        ident[0:TURN, 0:TURN])
                last.then_inc(chain_done, 1)
            elif name == "mean":
                pe.wait_ge(chain_done, chained(i, kind, step) - 1)
                if half == 0:
                    for g in (GROUPS - 2, GROUPS - 1):
                        pe.wait_ge(y_loaded[kind - 1][g % 2], load_count(i - 1, kind - 1, g))
                    pe.matmul(ps_r[:, 0:LENGTHS[kind]], skip[:, kind - 1, :], kept[kind][:, :],
                              start=True, stop=False)
                for c in range(half, min(half + MEAN, SEGS[kind - 1])):
                    rows = min(SEG, 2 * LENGTHS[kind] - c * SEG)
                    a = c * SEG // 2
                    last = pe.matmul(ps_r[:, a:a + rows // 2],
                                     y_nat[kind - 1][0:rows, c, :, :].rearrange("q b e -> q (b e)"),
                                     halver[0:rows, 0:rows // 2], start=False, stop=c == SEGS[kind - 1] - 1)
                last.then_inc(chain_done, 1)
            elif name == "z":
                pe.wait_ge(chain_done, chained(i, kind, step) - 1)
                a, b = HALVES[kind][half]
                pe.matmul(ps_r[:, 0:b - a], w_delta[:, kind, :], xT[kind][:, a:b], start=True, stop=True)\
                  .then_inc(chain_done, 1)
            elif name == "b":
                pe.wait_ge(chain_done, chained(i, kind, step) - 1)
                a, b = HALVES[kind][half]
                pe.matmul(ps_r[:, 0:b - a], w_state[:, kind, 0, :], xT[kind][:, a:b], start=True, stop=True)\
                  .then_inc(chain_done, 1)
            elif name == "c":
                pe.wait_ge(chain_done, chained(i, kind, step) - 1)
                a, b = WIDE[kind][half]
                pe.matmul(ps_r[:, 0:b - a], w_state[:, kind, 1, :], xT[kind][:, a:b], start=True, stop=True)\
                  .then_inc(chain_done, 1)
            elif name == "last":
                pe.wait_ge(chain_done, chained(i, kind, step) - 1)
                for g in (GROUPS - 2, GROUPS - 1):
                    pe.wait_ge(y_loaded[2][g % 2], load_count(i - 1, 2, g))
                for c in range(SEGS[2]):
                    rows = min(SEG, LENGTHS[2] - c * SEG)
                    to = ps_r[0:rows, 128 * c:128 * c + 128]
                    pe.matmul(to, xT[2][:, c * SEG:c * SEG + rows], skip[:, 2, :], start=True, stop=False)
                    last = pe.matmul(to, ident[0:rows, 0:rows],
                                     y_nat[2][0:rows, c, :, :].rearrange("q b e -> q (b e)"), start=False, stop=True)
                last.then_inc(chain_done, 1)

        for step in CHAINS[0]:
            chain_step(-1, 0, step)

        def spread(to, stage, s, v):
            n = LENGTHS[stage]
            for j, col in enumerate(feature_columns(stage)):
                q, r = divmod(s * EPS[stage] + j, GE)
                for a, b in (((0, 512), (512, n)) if stage == 0 else ((0, n),)):
                    last = pe.matmul(to[:, col + a:col + b], pick[:, r, :], stack[stage][:, v, q, a:b],
                                     start=True, stop=True)
            return last

        def spread_u(i, stage, s):
            if s == 0:
                pe.wait_ge(chain_done, operands_count(i, stage))
                if due(count := stacks_before(i, "keep2" if stage == 0 else "keep1") * (16 * STACK_DMAS)):
                    pe.wait_ge(stacked, count)
            if due(count := before(i, stage, STEPS) + s):
                pe.wait_ge(u_copied, count)
            spread(ps_u[:, :], stage, s, 1).then_inc(u_ready, 1)

        def spread_delta(i, stage, s):
            if due(count := before(i, stage, STEPS) + s - 1):
                pe.wait_ge(scanned, count)
            spread(ps_d[:, s % 2, :], stage, s, 0).then_inc(d_ready, 1)

        def segment(i, stage, g, c):
            if c == 0:
                pe.wait_ge(scanned, before(i, stage, STEPS) + (g + 1) * SPG[stage])
            if c % 2 == 0:
                if due(count := bank_count(i, stage, g, c // 2)):
                    pe.wait_ge(y_copied, count)
            states = h[:, g % 2, 0:GE * PADDED[stage]].rearrange("p (e l) -> p e l", e=GE)
            for t in range(4):
                piece = 4 * c + t
                last = pe.matmul(ps_y[32 * t:32 * t + 32, 256 * (c % 2):256 * (c % 2) + 256],
                                 c_out[stage][:, piece, :, :].rearrange("p b l -> p (b l)"),
                                 states[:, :, CH * piece:CH * piece + CH], start=True, stop=True)
            if c % 2 == 1 or c == SEGS[stage] - 1:
                last.then_inc(y_ready, 1)

        def iteration(i):
            for what in iteration_plan(i):
                if what[0] == "main":
                    spread_delta(i, what[1], what[2])
                elif what[0] == "feed":
                    spread_u(i - what[2], what[1], what[3])
                elif what[0] == "seg":
                    _, stage, lag, g, c = what
                    segment(i - lag, stage, g, c)
                else:
                    chain_step(i, what[1], what[2])

        everywhere(pe, iteration)



TOKENS = LENGTHS[2]
HALF = 94
REST = TOKENS - HALF
HEADS, HEAD = 4, 16
ROWS = 32
MAX_REL = 30
REL = 2 * MAX_REL + 1
SPREAD = TOKENS + HALF - 1
FIRST_REL = (HALF - 1, 2 * HALF - 1)
EXPERTS, HIDDEN = 16, 128
BLOCK = 2 * TOKENS
TILES, TILE = 3, 125
LAST_TILE = BLOCK - (TILES - 1) * TILE
RING = 4
LN_EPS = 1e-5

NORMALISE = [("features", 1, 0.3), ("centre", 1, 0.3), ("square", 1, 0.3), ("squares", 1, 0.3),
             ("variance", 1, 0.2), ("root", 1, 0.9), ("scale", 1, 0.3)]

ATTENTION = [
    [("load", 32, 2.3)],
    NORMALISE + NORMALISE + [("turn", 1, 0.8), ("affine", 1, 0.5)],
    [("q", 1, 1.5), ("q_out", 1, 0.9), ("rel", 1, 0.9), ("rel_out", 1, 0.9), ("fill", 1, 2.5), ("kv", 1, 1.3),
     ("kv_out", 1, 0.8)],
    [("store_rel", 32, 3.0), ("load_pos", 64, 3.0)],
    [(("qk", c), 1, 2.6) for c in range(2)] + [("add", 1, 1.7), ("top", 1, 1.7), ("shift", 1, 0.2)]
    + [(("exp", h), 1, 0.9) for h in range(HEADS)],
    [("inverse", 1, 0.2), ("divide", 1, 1.8)]
    + [((what, c, half), 1, 0.8) for c in range(2) for half in range(2) for what in ("probs", "probs_out")]
    + [("context", 1, 1.3), ("context_out", 1, 0.4), ("w_o", 1, 0.5), ("sum", 1, 0.3)],
    [("store", 32, 2.3)]]
RANKING = ("best", "equal", "rank", "lowest", "mark", "without")
EXPERT = [
    [("load", 32, 2.3)],
    NORMALISE + [("turn", 1, 0.9), ("turned", 1, 1.2), ("less_high", 1, 1.0), ("middle", 1, 0.8), ("low", 1, 0.5)],
    [("logits", 1, 0.4), ("logits_out", 1, 0.3)]
    + [((what, r), 1, 0.35) for r in range(2) for what in RANKING if (what, r) != ("without", 1)]
    + [("margin", 1, 0.3), ("odds", 1, 0.3), ("one_more", 1, 0.3), ("first_share", 1, 0.3), ("shares", 1, 0.3),
       ("weigh", 1, 0.3), ("mix", 1, 0.3), ("turn_mix", 1, 0.9), ("mix_turned", 1, 0.5), ("b2", 1, 0.8),
       ("begin", 1, 0.4)],
    [(("pair", p), 2, 1.9) for p in range(EXPERTS // 2)],
    NORMALISE + [("gamma", 1, 0.4), ("beta", 1, 0.4), ("sum", 1, 0.4)],
    [("store", 32, 2.3)]]


def chain_length(chain):
    return sum(weight for _, weight, _ in chain)


def count_before(chains, k, n, piece):
    return piece * chain_length(chains[k]) + sum(weight for _, weight, _ in chains[k][:n])


def count_through(chains, k, piece):
    return (piece + 1) * chain_length(chains[k])


def chains_order(chains):
    begins = [(sum(extent for _, _, extent in chain[:n]), k, n) for k, chain in enumerate(chains)
              for n in range(len(chain))]
    return [(k, n) for _, k, n in sorted(begins)]


def walk(eng, chains, pieces, do):
    order = chains_order(chains)

    def iteration(i, place, j=None):
        for k, n in order:
            if not isinstance(i, int) or 0 <= i - k < pieces:
                turn = i // RING if isinstance(i, int) else j
                turn, at = turn + (place - k) // RING, (place - k) % RING
                do(k, n, chains[k][n][0], i - k, at, turn)

    full = -(-(len(chains) - 1 + RING) // RING)
    for i in range(full * RING):
        iteration(i, i % RING)
    with eng.Fori(full, pieces // RING) as j:
        for place in range(RING):
            iteration(j * RING + place, place, j)
    for i in range(pieces, pieces + len(chains) - 1):
        iteration(i, i % RING)


def normalise_step(dve, name, before, done, x, xc, square, total):
    wide = total[:, :, None].to_broadcast(list(x.shape))
    if name == "features":
        dve.tensor_reduce(total, x, mybir.AxisListType.X, ALU.add).then_inc(done, 1)
    elif name == "centre":
        dve.wait_ge(done, before)
        dve.scalar_tensor_tensor(xc, wide, -1.0 / E, x, ALU.mult, ALU.add).then_inc(done, 1)
    elif name == "square":
        dve.wait_ge(done, before)
        dve.tensor_tensor(square, xc, xc, ALU.mult).then_inc(done, 1)
    elif name == "squares":
        dve.wait_ge(done, before)
        dve.tensor_reduce(total, square, mybir.AxisListType.X, ALU.add).then_inc(done, 1)
    elif name == "variance":
        dve.wait_ge(done, before)
        dve.tensor_scalar(total, total, 1.0 / E, LN_EPS, ALU.mult, ALU.add).then_inc(done, 1)
    elif name == "scale":
        dve.wait_ge(done, before)
        dve.tensor_tensor(xc, xc, wide, ALU.mult).then_inc(done, 1)


def attention(nc, ctx, weights, hidden, spread, attended):
    def sb(name, shape, dt=F32):
        return ctx.enter_context(nc.sbuf_tensor(name, shape, dt))

    def ps(name, shape):
        return ctx.enter_context(nc.psum_tensor(name, shape, F32))

    def sem(name):
        return ctx.enter_context(nc.semaphore(name))

    ident = sb("ident_att", [128, 128])
    w_q = sb("w_q", [E + 2, 2, HEADS * ROWS])
    w_k = sb("w_k", [E + 1, HEADS * ROWS])
    w_v = sb("w_v", [E + 1, HEADS * ROWS])
    w_o = sb("w_o", [HEADS * ROWS, E])
    w_pos = sb("w_pos", [E + 1, HEADS * ROWS])
    enc = sb("enc", [E + 1, REL])
    affine = sb("affine", [E, 2])
    p_pos = sb("p_pos", [HEADS * ROWS, HEADS, REL])
    spare = sb("spare", [HEADS * ROWS, 1])
    nothing = sb("nothing", [HALF, HEADS])
    power = sb("power", [HALF, 2])
    hx = sb("hx", [HALF, RING, 2, E])
    root = sb("root", [HALF, 2])
    square = sb("square", [HALF, 2, E])
    xc = sb("xc", [HALF, 2, E])
    xn = sb("xn", [HALF, 2, E])
    xT = sb("xT_att", [E + 2, RING, 2 * HALF])
    q_v = sb("q_v", [HEADS * ROWS, 2 * HALF])
    q_u = sb("q_u", [HEADS * ROWS, RING, 2 * HALF])
    kT = sb("kT", [HEADS * ROWS, RING, TOKENS])
    v = sb("v", [HALF, RING, 2, HEADS * ROWS])
    rel_sc = sb("rel_sc", [HALF, RING, 2, HEADS, SPREAD])
    pos = sb("pos", [HALF, RING, HEADS, 2, TOKENS])
    scores = sb("scores", [HALF, RING, HEADS, 2, TOKENS])
    top = sb("top", [HALF, HEADS, 2])
    sums = sb("sums", [HALF, RING, HEADS, 2])
    inverse = sb("inverse", [HALF, HEADS, 2])
    probsT = sb("probsT", [HALF, 2, HEADS, 2, HALF])
    contextT = sb("contextT", [HEADS * ROWS, 2 * HALF])
    residual = sb("residual", [HALF, RING, 2, E])
    result = sb("result", [HALF, RING, 2, E])
    ps_x = ps("ps_x", [128, 512])
    ps_q = ps("ps_q", [128, 512])
    ps_s = ps("ps_s", [128, HEADS, 512])
    ps_t = ps("ps_t", [128, 512])
    ps_c = ps("ps_c", [128, 512])

    weights_in = sem("att_weights_in")
    ones = sem("att_ones")
    constant = sem("att_constant")
    encoded = sem("encoded")
    encoding_out = sem("encoding_out")
    normal_done, project_done, skew_done, score_done, output_done = \
        [sem(name) for name in ("normal_done", "project_done", "skew_done", "score_done", "output_done")]
    loaded = [sem(f"loaded_att{p}") for p in range(RING)]
    stored = [sem(f"stored_att{p}") for p in range(RING)]
    chains = ATTENTION
    quarter = 1.0 / HEAD ** 0.5

    def halves(dram):
        return dram[0:HALF, :], dram[HALF:TOKENS, :]

    block = ctx.enter_context(nc.Block())

    @block.sync
    def _(sp):
        for name, dst in (("ident", ident), ("w_q", w_q), ("w_k", w_k), ("w_v", w_v), ("w_o", w_o),
                          ("w_pos", w_pos), ("enc", enc), ("affine", affine), ("spare", spare)):
            sp.dma_start(dst[tuple(slice(None) for _ in dst.shape)], weights[name]).then_inc(weights_in, 16)
        sp.wait_ge(ones, 1)

        def do(k, n, name, b, place, turn):
            if name == "load":
                first, second = halves(hidden[b])
                if due(count := count_through(chains, 1, b - RING)):
                    sp.wait_ge(normal_done, count)
                sp.dma_start(hx[:, place, 0, :], first).then_inc(loaded[place], 16)
                sp.dma_start(hx[0:REST, place, 1, :], second).then_inc(loaded[place], 16)
            elif name == "store_rel":
                made = fixed(sp, count_through(chains, 2, b))
                read = fixed(sp, count_before(chains, 3, 0, b))
                sp.wait_ge(project_done, made)
                if due(read):
                    sp.wait_ge(skew_done, read)
                for c in range(2):
                    sp.dma_start(spread[c], rel_sc[:, place, c, :, :]).then_inc(skew_done, 16)
            elif name == "load_pos":
                first, second = halves(hidden[b])
                written = fixed(sp, count_before(chains, 3, n, b))
                scored = fixed(sp, count_through(chains, 4, b - RING))
                output = fixed(sp, count_through(chains, 5, b - RING))
                sp.wait_ge(skew_done, written)
                if due(scored):
                    sp.wait_ge(score_done, scored)
                    sp.wait_ge(output_done, output)
                for c in range(2):
                    skewed = bass.AP(tensor=spread[c].tensor, offset=spread[c].offset + HALF - 1,
                                     ap=[[HEADS * SPREAD - 1, HALF], [SPREAD, HEADS], [1, TOKENS]])
                    sp.dma_start(pos[:, place, :, c, :], skewed).then_inc(skew_done, 16)
                sp.dma_start(residual[:, place, 0, :], first).then_inc(skew_done, 16)
                sp.dma_start(residual[0:REST, place, 1, :], second).then_inc(skew_done, 16)
            elif name == "store":
                first, second = halves(attended[b])
                sp.wait_ge(output_done, count_through(chains, 5, b))
                sp.dma_start(first, result[:, place, 0, :]).then_inc(stored[place], 16)
                sp.dma_start(second, result[0:REST, place, 1, :]).then_inc(stored[place], 16)

        walk(sp, chains, BATCH, do)
        for place in range(RING):
            sp.wait_ge(stored[place], 32 * BATCH // RING)

    @block.scalar
    def _(act):
        act.wait_ge(weights_in, 16 * 9)
        act.wait_ge(encoded, 1)
        act.wait_ge(ones, 1)
        for h in range(HEADS):
            rows = slice(h * ROWS, (h + 1) * ROWS)
            act.activation(p_pos[rows, h, :], ps_x[rows, 0:REL], ACT.Copy).then_inc(encoding_out, 1)

        def do(k, n, name, b, place, turn):
            before = count_before(chains, k, n, b)
            if name == "affine":
                act.wait_ge(normal_done, before)
                if due(count := count_through(chains, 2, b - RING)):
                    act.wait_ge(project_done, count)
                act.activation(xT[0:E, place, :], ps_x[0:E, 0:2 * HALF], ACT.Identity,
                               scale=affine[:, 0:1], bias=affine[:, 1:2]).then_inc(normal_done, 1)
            elif name == "q_out":
                act.wait_ge(project_done, before)
                if due(count := count_through(chains, 4, b - RING)):
                    act.wait_ge(score_done, count)
                act.activation(q_v[:, :], ps_q[:, 0:2 * HALF], ACT.Copy)
                act.activation(q_u[:, place, :], ps_q[:, 2 * HALF:4 * HALF], ACT.Copy).then_inc(project_done, 1)
            elif name == "rel_out":
                act.wait_ge(project_done, before)
                if due(count := count_through(chains, 3, b - RING)):
                    act.wait_ge(skew_done, count)
                for c in range(2):
                    a = FIRST_REL[c] - MAX_REL
                    last = act.activation(
                        rel_sc[:, place, c, :, a:a + REL],
                        ps_q[0:HALF, c * HEADS * REL:(c + 1) * HEADS * REL].rearrange("p (h r) -> p h r", h=HEADS),
                        ACT.Copy)
                last.then_inc(project_done, 1)
            elif name[0] == "exp":
                h = name[1]
                act.wait_ge(score_done, before)
                for c in range(2):
                    rows = scores[:, place, h, c, :]
                    last = act.activation(rows, rows, ACT.Exp, scale=quarter, bias=top[:, h, c:c + 1],
                                          accum_out=sums[:, place, h, c:c + 1])
                last.then_inc(score_done, 1)
            elif name[0] == "probs_out":
                _, c, half = name
                act.wait_ge(output_done, before)
                keys = HALF if half == 0 else REST
                act.activation(probsT[0:keys, half, :, c, :],
                               ps_t[0:keys, 0:HEADS * HALF].rearrange("p (h t) -> p h t", h=HEADS), ACT.Copy)\
                   .then_inc(output_done, 1)
            elif name == "context_out":
                act.wait_ge(output_done, before)
                act.activation(contextT[:, :], ps_c[:, 0:2 * HALF], ACT.Identity, bias=spare[:, 0:1])\
                   .then_inc(output_done, 1)

        walk(act, chains, BATCH, do)

    @block.vector
    def _(dve):
        dve.memset(xT[E:E + 2, :, :], 1.0)
        dve.memset(p_pos[:, :, :], 0.0)
        dve.memset(hx[:, :, 1, :], 0.0)
        dve.memset(residual[:, :, 1, :], 0.0).then_inc(ones, 1)

        def do(k, n, name, b, place, turn):
            before = count_before(chains, k, n, b)
            if k == 1:
                if n == 0:
                    dve.wait_ge(loaded[place], 32 * turn + 32)
                    if due(before):
                        dve.wait_ge(normal_done, before)
                elif name == "features":
                    dve.wait_ge(normal_done, before)
                frm, to = (hx[:, place, :, :], xc[:, :, :]) if n < len(NORMALISE) else (xc[:, :, :], xn[:, :, :])
                normalise_step(dve, name, before, normal_done, frm, to, square[:, :, :], root[:, :])
            elif name == "kv_out":
                dve.wait_ge(project_done, before)
                if due(count := count_through(chains, 5, b - RING)):
                    dve.wait_ge(output_done, count)
                dve.tensor_copy(kT[:, place, :], ps_q[:, 0:TOKENS])
                dve.tensor_copy(v[:, place, :, :].rearrange("p c e -> p (c e)"),
                                ps_q[0:HALF, 2 * HALF:2 * HALF + 2 * HEADS * ROWS]).then_inc(project_done, 1)
            elif name == "add":
                dve.wait_ge(score_done, before)
                dve.wait_ge(skew_done, count_through(chains, 3, b))
                if due(count := count_through(chains, 5, b - RING)):
                    dve.wait_ge(output_done, count)
                dve.tensor_tensor(scores[:, place, :, :, :].rearrange("p h c s -> p h (c s)"),
                                  ps_s[0:HALF, :, 0:2 * TOKENS],
                                  pos[:, place, :, :, :].rearrange("p h c s -> p h (c s)"), ALU.add)\
                   .then_inc(score_done, 1)
            elif name == "top":
                dve.wait_ge(score_done, before)
                dve.tensor_reduce(top[:, :, :].rearrange("p h c -> p (h c)"),
                                  scores[:, place, :, :, :].rearrange("p h c s -> p (h c) s"),
                                  mybir.AxisListType.X, ALU.max).then_inc(score_done, 1)
            elif name == "shift":
                dve.wait_ge(score_done, before)
                dve.tensor_scalar(top[:, :, :], top[:, :, :], -quarter, None, ALU.mult).then_inc(score_done, 1)
            elif name == "inverse":
                dve.wait_ge(score_done, count_through(chains, 4, b))
                if due(before):
                    dve.wait_ge(output_done, before)
                dve.reciprocal(inverse[:, :, :], sums[:, place, :, :]).then_inc(output_done, 1)
            elif name == "divide":
                dve.wait_ge(output_done, before)
                probs = scores[:, place, :, :, :].rearrange("p h c s -> p (h c) s")
                over = inverse[:, :, :].rearrange("p h c -> p (h c)")[:, :, None]
                dve.tensor_tensor(probs, probs, over.to_broadcast([HALF, 2 * HEADS, TOKENS]), ALU.mult)\
                   .then_inc(output_done, 1)
            elif k == 5 and name == "sum":
                dve.wait_ge(output_done, before)
                if due(32 * turn):
                    dve.wait_ge(stored[place], 32 * turn)
                dve.tensor_tensor(result[:, place, :, :].rearrange("p c e -> p (c e)"), ps_c[0:HALF, 256:256 + 2 * E],
                                  residual[:, place, :, :].rearrange("p c e -> p (c e)"), ALU.add)\
                   .then_inc(output_done, 1)

        walk(dve, chains, BATCH, do)

    @block.gpsimd
    def _(pool):
        pool.memset(nothing[:, :], 0.0)
        pool.memset(power[:, :], -0.5).then_inc(constant, 1)
        pool.wait_ge(constant, 1)

        def do(k, n, name, b, place, turn):
            before = count_before(chains, k, n, b)
            if name == "root":
                pool.wait_ge(normal_done, before)
                pool.tensor_tensor(root[:, :], root[:, :], power[:, :], ALU.pow).then_inc(normal_done, 1)
            elif name == "fill":
                pool.wait_ge(project_done, before)
                for c in range(2):
                    a = FIRST_REL[c] - MAX_REL
                    z = a + REL
                    for first, end, edge in ((0, a, a), (z, SPREAD, z - 1)):
                        wide = [HALF, HEADS, end - first]
                        last = pool.tensor_tensor(rel_sc[:, place, c, :, first:end],
                                                  rel_sc[:, place, c, :, edge:edge + 1].to_broadcast(wide),
                                                  nothing[:, :, None].to_broadcast(wide), ALU.add)
                last.then_inc(project_done, 1)

        walk(pool, chains, BATCH, do)

    @block.tensor
    def _(pe):
        pe.wait_ge(weights_in, 16 * 9)
        pe.wait_ge(ones, 1)
        pe.matmul(ps_x[:, 0:REL], w_pos[:, :], enc[:, :], start=True, stop=True).then_inc(encoded, 1)
        pe.wait_ge(encoding_out, HEADS)

        def tile(c):
            return slice(c * HALF, (c + 1) * HALF)

        def head(h):
            return slice(h * ROWS, (h + 1) * ROWS)

        def do(k, n, name, b, place, turn):
            before = count_before(chains, k, n, b)
            if name == "turn":
                pe.wait_ge(normal_done, before)
                for c in range(2):
                    last = pe.matmul(ps_x[0:E, tile(c)], xn[:, c, :], ident[0:HALF, 0:HALF], start=True, stop=True)
                last.then_inc(normal_done, 1)
            elif name == "q":
                pe.wait_ge(normal_done, count_through(chains, 1, b))
                if due(before):
                    pe.wait_ge(project_done, before)
                for j in range(2):
                    last = pe.matmul(ps_q[:, 2 * j * HALF:2 * (j + 1) * HALF], w_q[:, 1 - j, :], xT[:, place, :],
                                     start=True, stop=True)
                last.then_inc(project_done, 1)
            elif name == "rel":
                pe.wait_ge(project_done, before)
                for c in range(2):
                    a = c * HEADS * REL
                    last = pe.matmul(ps_q[0:HALF, a:a + HEADS * REL], q_v[:, tile(c)],
                                     p_pos[:, :, :].rearrange("p h r -> p (h r)"), start=True, stop=True)
                last.then_inc(project_done, 1)
            elif name == "kv":
                pe.wait_ge(project_done, before)
                pe.matmul(ps_q[:, 0:TOKENS], w_k[:, :], xT[0:E + 1, place, 0:TOKENS], start=True, stop=True)
                for c in range(2):
                    a = 2 * HALF + c * HEADS * ROWS
                    last = pe.matmul(ps_q[0:HALF, a:a + HEADS * ROWS], xT[0:E + 1, place, tile(c)], w_v[:, :],
                                     start=True, stop=True)
                last.then_inc(project_done, 1)
            elif name[0] == "qk":
                c = name[1]
                pe.wait_ge(project_done, count_through(chains, 2, b))
                if due(before):
                    pe.wait_ge(score_done, before)
                for h in range(HEADS):
                    last = pe.matmul(ps_s[0:HALF, h, c * TOKENS:(c + 1) * TOKENS], q_u[head(h), place, tile(c)],
                                     kT[head(h), place, :], start=True, stop=True)
                last.then_inc(score_done, 1)
            elif name[0] == "probs":
                _, c, half = name
                pe.wait_ge(output_done, before)
                a, keys = half * HALF, HALF if half == 0 else REST
                for h in range(HEADS):
                    last = pe.transpose(ps_t[0:keys, tile(h)], scores[:, place, h, c, a:a + keys],
                                        ident[0:HALF, 0:HALF])
                last.then_inc(output_done, 1)
            elif name == "context":
                pe.wait_ge(output_done, before)
                for half, keys in ((0, HALF), (1, REST)):
                    for h in range(HEADS):
                        last = pe.matmul(ps_c[head(h), 0:2 * HALF], v[0:keys, place, half, h * ROWS:(h + 1) * ROWS],
                                         probsT[0:keys, half, h, :, :].rearrange("p c t -> p (c t)"),
                                         start=half == 0, stop=half == 1)
                last.then_inc(output_done, 1)
            elif name == "w_o":
                pe.wait_ge(output_done, before)
                for c in range(2):
                    last = pe.matmul(ps_c[0:HALF, 256 + c * E:256 + (c + 1) * E], contextT[:, tile(c)], w_o[:, :],
                                     start=True, stop=True)
                last.then_inc(output_done, 1)

        walk(pe, chains, BATCH, do)


def experts(nc, ctx, weights, attended, out):
    def sb(name, shape, dt=F32):
        return ctx.enter_context(nc.sbuf_tensor(name, shape, dt))

    def ps(name, shape):
        return ctx.enter_context(nc.psum_tensor(name, shape, F32))

    def sem(name):
        return ctx.enter_context(nc.semaphore(name))

    pairs = EXPERTS // 2
    ident = sb("ident_ffn", [128, 128])
    w1 = sb("w1", [2 * E, EXPERTS * HIDDEN])
    w1_parts = sb("w1_parts", [2 * E, 3, EXPERTS * HIDDEN], BF16)
    b1 = sb("b1", [HIDDEN, EXPERTS])
    w2 = sb("w2", [HIDDEN, EXPERTS, E])
    b2 = sb("b2", [EXPERTS, E])
    gate = sb("gate", [E, EXPERTS])
    gate_b = sb("gate_b", [TILE, EXPERTS])
    ranks = sb("ranks", [TILE, EXPERTS])
    gamma = sb("gamma", [TILE, E])
    beta = sb("beta", [TILE, E])
    power = sb("power_ffn", [TILE, TILES])
    hx = sb("hx_ffn", [TILE, RING, TILES, E])
    square = sb("square_ffn", [TILE, 2, TILES, E])
    root = sb("root_ffn", [TILE, 2, TILES])
    xn = sb("xn_ffn", [TILE, RING, TILES, E])
    xT = sb("xT_ffn", [E, RING, TILES * TILE])
    left = sb("left", [2 * E, TILES * TILE])
    middle = sb("middle", [E, TILES * TILE], BF16)
    x_parts = sb("x_parts", [2 * E, RING, 2, TILES * TILE], BF16)
    logits = sb("logits", [TILE, TILES, EXPERTS])
    best = sb("best", [TILE, 2, TILES])
    equal = sb("equal", [TILE, TILES, EXPERTS])
    lowest = sb("lowest", [TILE, TILES])
    mark = sb("mark", [TILE, 2, TILES, EXPERTS])
    share = sb("share", [TILE, 2, TILES])
    mix = sb("mix", [TILE, RING, TILES, EXPERTS])
    mixT = sb("mixT", [EXPERTS, TILES * TILE])
    total = sb("total", [TILE, RING, TILES, E])
    active = sb("active", [HIDDEN, 2, 2, TILES * TILE])
    result = sb("result_ffn", [TILE, RING, TILES, E])
    ps_x = ps("ps_x_ffn", [128, 512])
    ps_g = ps("ps_g", [128, 512])
    ps_h = ps("ps_h", [HIDDEN, 2, 2, 512])
    ps_o = ps("ps_o", [128, 2, 512])

    weights_in = sem("ffn_weights_in")
    ones = sem("ffn_ones")
    constant = sem("ffn_constant")
    split = sem("w1_split")
    hidden_ready = sem("hidden_ready")
    hidden_active = sem("hidden_active")
    pair_ready = sem("pair_ready")
    token_done, gate_done, pair_done, finish_done = \
        [sem(name) for name in ("token_done", "gate_done", "pair_done", "finish_done")]
    loaded = [sem(f"loaded_ffn{p}") for p in range(RING)]
    stored = [sem(f"stored_ffn{p}") for p in range(RING)]
    chains = EXPERT
    blocks = BATCH * TOKENS // BLOCK
    wide = [TILE, TILES, EXPERTS]

    def parts(dram, blk):
        full = (TILES - 1) * TILE
        rows = dram[blk]
        return rows[0:full, :].rearrange("(c p) e -> p c e", p=TILE), rows[full:BLOCK, :]

    def tile(c):
        return slice(c * TILE, (c + 1) * TILE)

    block = ctx.enter_context(nc.Block())

    @block.sync
    def _(sp):
        for name, dst in (("ident", ident), ("w1", w1), ("b1", b1), ("w2", w2), ("b2", b2), ("gate", gate),
                          ("gate_b", gate_b), ("ranks", ranks), ("gamma", gamma), ("beta", beta)):
            sp.dma_start(dst[tuple(slice(None) for _ in dst.shape)], weights[name]).then_inc(weights_in, 16)
        sp.wait_ge(ones, 1)

        def do(k, n, name, blk, place, turn):
            if name == "load":
                first, last = parts(attended, blk)
                if due(count := count_through(chains, 4, blk - RING)):
                    sp.wait_ge(finish_done, count)
                sp.dma_start(hx[:, place, 0:TILES - 1, :], first).then_inc(loaded[place], 16)
                sp.dma_start(hx[0:LAST_TILE, place, TILES - 1, :], last).then_inc(loaded[place], 16)
            elif name == "store":
                first, last = parts(out, blk)
                sp.wait_ge(finish_done, count_through(chains, 4, blk))
                sp.dma_start(first, result[:, place, 0:TILES - 1, :]).then_inc(stored[place], 16)
                sp.dma_start(last, result[0:LAST_TILE, place, TILES - 1, :]).then_inc(stored[place], 16)

        walk(sp, chains, blocks, do)
        for place in range(RING):
            sp.wait_ge(stored[place], 32 * blocks // RING)

    @block.scalar
    def _(act):
        act.wait_ge(weights_in, 16 * 10)

        def do(k, n, name, blk, place, turn):
            before = count_before(chains, k, n, blk)
            if name[0] == "pair":
                act.wait_ge(hidden_ready, blk * pairs + n + 1)
                if due(count := blk * pairs + n - 1):
                    act.wait_ge(pair_ready, count)
                for j in range(2):
                    e = 2 * n + j
                    last = act.activation(active[:, n % 2, j, :], ps_h[:, n % 2, j, 0:TILES * TILE], ACT.Relu,
                                          bias=b1[:, e:e + 1])
                last.then_inc(hidden_active, 1)
            elif name == "turned":
                act.wait_ge(token_done, before)
                if due(count := count_through(chains, 3, blk - RING)):
                    act.wait_ge(pair_done, count)
                act.activation(xT[:, place, :], ps_x[0:E, 0:TILES * TILE], ACT.Copy)
                act.activation(x_parts[0:E, place, 0, :], ps_x[0:E, 0:TILES * TILE], ACT.Copy)
                act.activation(x_parts[E:2 * E, place, 1, :], ps_x[E:2 * E, 0:TILES * TILE], ACT.Copy)\
                   .then_inc(token_done, 1)
            elif name == "middle":
                act.wait_ge(token_done, before)
                act.activation(middle[:, :], left[0:E, :], ACT.Copy)
                act.activation(x_parts[E:2 * E, place, 0, :], left[E:2 * E, :], ACT.Copy).then_inc(token_done, 1)
            elif name == "odds":
                act.wait_ge(gate_done, before)
                act.activation(share[:, 1, :], share[:, 1, :], ACT.Exp).then_inc(gate_done, 1)
            elif name == "mix_turned":
                act.wait_ge(gate_done, before)
                act.activation(mixT[:, :], ps_g[0:EXPERTS, 0:TILES * TILE], ACT.Copy).then_inc(gate_done, 1)

        walk(act, chains, blocks, do)

    @block.vector
    def _(dve):
        dve.memset(hx[:, :, TILES - 1, :], 0.0).then_inc(ones, 1)
        dve.wait_ge(weights_in, 16 * 10)
        high, mid, last_part = w1_parts[:, 0, :], w1_parts[:, 1, :], w1_parts[E:2 * E, 2, :]
        dve.tensor_copy(high, w1[:, :]).then_inc(split, 1)
        dve.wait_ge(split, 1)
        dve.tensor_copy(w1_parts[0:E, 2, :], w1_parts[0:E, 0, :])
        dve.tensor_tensor(w1[:, :], w1[:, :], high, ALU.subtract).then_inc(split, 1)
        dve.wait_ge(split, 2)
        dve.tensor_copy(mid, w1[:, :]).then_inc(split, 1)
        dve.wait_ge(split, 3)
        dve.tensor_tensor(last_part, w1[E:2 * E, :], w1_parts[E:2 * E, 1, :], ALU.subtract).then_inc(split, 1)

        def do(k, n, name, blk, place, turn):
            before = count_before(chains, k, n, blk)
            if k == 1 and n < len(NORMALISE):
                if n == 0:
                    dve.wait_ge(loaded[place], 32 * turn + 32)
                    if due(before):
                        dve.wait_ge(token_done, before)
                    if due(count := count_through(chains, 2, blk - RING)):
                        dve.wait_ge(gate_done, count)
                normalise_step(dve, name, before, token_done, hx[:, place, :, :], xn[:, place, :, :], square[:, 0, :, :],
                               root[:, 0, :])
            elif name == "less_high":
                dve.wait_ge(token_done, before)
                dve.tensor_tensor(left[0:E, :], ps_x[0:E, 0:TILES * TILE], x_parts[0:E, place, 0, :], ALU.subtract)
                dve.tensor_tensor(left[E:2 * E, :], ps_x[E:2 * E, 0:TILES * TILE], x_parts[E:2 * E, place, 1, :],
                                  ALU.subtract).then_inc(token_done, 1)
            elif name == "low":
                dve.wait_ge(token_done, before)
                dve.tensor_tensor(x_parts[0:E, place, 1, :], left[0:E, :], middle[:, :], ALU.subtract)\
                   .then_inc(token_done, 1)
            elif name == "logits_out":
                dve.wait_ge(gate_done, before)
                dve.tensor_tensor(logits[:, :, :], ps_g[0:TILE, 0:TILES * EXPERTS].rearrange("p (c e) -> p c e", c=TILES),
                                  gate_b[:, None, :].to_broadcast(wide), ALU.add).then_inc(gate_done, 1)
            elif name[0] == "best":
                dve.wait_ge(gate_done, before)
                dve.tensor_reduce(best[:, name[1], :], logits[:, :, :], mybir.AxisListType.X, ALU.max)\
                   .then_inc(gate_done, 1)
            elif name[0] == "equal":
                dve.wait_ge(gate_done, before)
                dve.tensor_tensor(equal[:, :, :], logits[:, :, :],
                                  best[:, name[1], :, None].to_broadcast(wide), ALU.is_equal).then_inc(gate_done, 1)
            elif name[0] == "rank":
                dve.wait_ge(gate_done, before)
                dve.tensor_tensor(equal[:, :, :], equal[:, :, :], ranks[:, None, :].to_broadcast(wide), ALU.mult)\
                   .then_inc(gate_done, 1)
            elif name[0] == "lowest":
                dve.wait_ge(gate_done, before)
                dve.tensor_reduce(lowest[:, :], equal[:, :, :], mybir.AxisListType.X, ALU.max).then_inc(gate_done, 1)
            elif name[0] == "mark":
                dve.wait_ge(gate_done, before)
                dve.tensor_tensor(mark[:, name[1], :, :], equal[:, :, :],
                                  lowest[:, :, None].to_broadcast(wide), ALU.is_equal).then_inc(gate_done, 1)
            elif name[0] == "without":
                dve.wait_ge(gate_done, before)
                dve.scalar_tensor_tensor(logits[:, :, :], mark[:, 0, :, :], -3e38, logits[:, :, :],
                                         ALU.mult, ALU.add).then_inc(gate_done, 1)
            elif name == "margin":
                dve.wait_ge(gate_done, before)
                dve.tensor_tensor(share[:, 1, :], best[:, 1, :], best[:, 0, :], ALU.subtract).then_inc(gate_done, 1)
            elif name == "one_more":
                dve.wait_ge(gate_done, before)
                dve.tensor_scalar(share[:, 0, :], share[:, 1, :], 1.0, None, ALU.add).then_inc(gate_done, 1)
            elif name == "first_share":
                dve.wait_ge(gate_done, before)
                dve.reciprocal(share[:, 0, :], share[:, 0, :]).then_inc(gate_done, 1)
            elif name == "shares":
                dve.wait_ge(gate_done, before)
                dve.tensor_tensor(share[:, 1, :], share[:, 1, :], share[:, 0, :], ALU.mult).then_inc(gate_done, 1)
            elif name == "weigh":
                dve.wait_ge(gate_done, before)
                marks = mark[:, :, :, :].rearrange("p r c e -> p (r c) e")
                shares = share[:, :, :].rearrange("p r c -> p (r c)")
                dve.tensor_tensor(marks, marks, shares[:, :, None].to_broadcast([TILE, 2 * TILES, EXPERTS]),
                                  ALU.mult).then_inc(gate_done, 1)
            elif name == "mix":
                dve.wait_ge(gate_done, before)
                if due(count := count_through(chains, 3, blk - RING)):
                    dve.wait_ge(pair_done, count)
                dve.tensor_tensor(mix[:, place, :, :], mark[:, 0, :, :], mark[:, 1, :, :], ALU.add)\
                   .then_inc(gate_done, 1)
            elif name == "begin":
                dve.wait_ge(gate_done, before)
                if due(count := count_through(chains, 4, blk - RING)):
                    dve.wait_ge(finish_done, count)
                dve.tensor_tensor(total[:, place, :, :].rearrange("p c e -> p (c e)"),
                                  xn[:, place, :, :].rearrange("p c e -> p (c e)"), ps_g[0:TILE, 0:TILES * E], ALU.add)\
                   .then_inc(gate_done, 1)
            elif name[0] == "pair":
                if n == 0:
                    dve.wait_ge(gate_done, count_through(chains, 2, blk))
                dve.wait_ge(pair_ready, blk * pairs + n + 1)
                for j in range(2):
                    if due(before + j):
                        dve.wait_ge(pair_done, before + j)
                    e = 2 * n + j
                    for c in range(TILES):
                        a = (j * TILES + c) * E
                        last = dve.scalar_tensor_tensor(total[:, place, c, :], ps_o[0:TILE, n % 2, a:a + E],
                                                        mix[:, place, c, e:e + 1], total[:, place, c, :],
                                                        ALU.mult, ALU.add)
                    last.then_inc(pair_done, 1)
            elif k == 4 and n < len(NORMALISE):
                if n == 0:
                    dve.wait_ge(pair_done, count_through(chains, 3, blk))
                    if due(before):
                        dve.wait_ge(finish_done, before)
                    if due(32 * turn):
                        dve.wait_ge(stored[place], 32 * turn)
                normalise_step(dve, name, before, finish_done, total[:, place, :, :], result[:, place, :, :],
                               square[:, 1, :, :], root[:, 1, :])
            elif name == "gamma":
                dve.wait_ge(finish_done, before)
                dve.tensor_tensor(result[:, place, :, :], result[:, place, :, :],
                                  gamma[:, None, :].to_broadcast([TILE, TILES, E]), ALU.mult).then_inc(finish_done, 1)
            elif name == "beta":
                dve.wait_ge(finish_done, before)
                dve.tensor_tensor(result[:, place, :, :], result[:, place, :, :],
                                  beta[:, None, :].to_broadcast([TILE, TILES, E]), ALU.add).then_inc(finish_done, 1)
            elif k == 4 and name == "sum":
                dve.wait_ge(finish_done, before)
                dve.tensor_tensor(result[:, place, :, :], result[:, place, :, :], hx[:, place, :, :], ALU.add)\
                   .then_inc(finish_done, 1)

        walk(dve, chains, blocks, do)

    @block.gpsimd
    def _(pool):
        pool.memset(power[:, :], -0.5).then_inc(constant, 1)
        pool.wait_ge(constant, 1)

        def do(k, n, name, blk, place, turn):
            before = count_before(chains, k, n, blk)
            if name == "root" and k == 1:
                pool.wait_ge(token_done, before)
                pool.tensor_tensor(root[:, 0, :], root[:, 0, :], power[:, :], ALU.pow).then_inc(token_done, 1)
            elif name == "root":
                pool.wait_ge(finish_done, before)
                pool.tensor_tensor(root[:, 1, :], root[:, 1, :], power[:, :], ALU.pow).then_inc(finish_done, 1)

        walk(pool, chains, blocks, do)

    @block.tensor
    def _(pe):
        pe.wait_ge(weights_in, 16 * 10)
        pe.wait_ge(ones, 1)
        pe.wait_ge(split, 4)

        def hidden_layers(pair, place, p):
            if due(count := pair - 1):
                pe.wait_ge(hidden_active, count)
            for j in range(2):
                e = 2 * p + j
                for part, of_x in ((0, 0), (1, 0), (2, 1)):
                    last = pe.matmul(ps_h[:, p % 2, j, 0:TILES * TILE],
                                     w1_parts[:, part, e * HIDDEN:(e + 1) * HIDDEN], x_parts[:, place, of_x, :],
                                     start=part == 0, stop=part == 2)
            last.then_inc(hidden_ready, 1)

        def do(k, n, name, blk, place, turn):
            before = count_before(chains, k, n, blk)
            if name[0] == "pair":
                if n == 0 and isinstance(blk, int) and blk == 0:
                    pe.wait_ge(token_done, count_through(chains, 1, blk))
                    hidden_layers(blk * pairs, place, 0)
                if n + 1 < pairs:
                    hidden_layers(blk * pairs + n + 1, place, n + 1)
                elif not isinstance(blk, int) or blk + 1 < blocks:
                    pe.wait_ge(token_done, count_through(chains, 1, blk + 1))
                    hidden_layers((blk + 1) * pairs, (place + 1) % RING, 0)
                pe.wait_ge(hidden_active, blk * pairs + n + 1)
                if due(count := before - 2):
                    pe.wait_ge(pair_done, count)
                for j in range(2):
                    for c in range(TILES):
                        a = (j * TILES + c) * E
                        last = pe.matmul(ps_o[0:TILE, n % 2, a:a + E], active[:, n % 2, j, tile(c)],
                                         w2[:, 2 * n + j, :], start=True, stop=True)
                last.then_inc(pair_ready, 1)
            elif name == "turn":
                pe.wait_ge(token_done, before)
                for c in range(TILES):
                    for j in range(2):
                        last = pe.matmul(ps_x[j * E:(j + 1) * E, tile(c)], xn[:, place, c, :], ident[0:TILE, 0:TILE],
                                         start=True, stop=True)
                last.then_inc(token_done, 1)
            elif name == "logits":
                pe.wait_ge(token_done, count_through(chains, 1, blk))
                if due(before):
                    pe.wait_ge(gate_done, before)
                for c in range(TILES):
                    last = pe.matmul(ps_g[0:TILE, c * EXPERTS:(c + 1) * EXPERTS], xT[:, place, tile(c)], gate[:, :],
                                     start=True, stop=True)
                last.then_inc(gate_done, 1)
            elif name == "turn_mix":
                pe.wait_ge(gate_done, before)
                for c in range(TILES):
                    last = pe.transpose(ps_g[0:EXPERTS, tile(c)], mix[:, place, c, :], ident[0:TILE, 0:TILE])
                last.then_inc(gate_done, 1)
            elif name == "b2":
                pe.wait_ge(gate_done, before)
                for c in range(TILES):
                    last = pe.matmul(ps_g[0:TILE, c * E:(c + 1) * E], mixT[:, tile(c)], b2[:, :],
                                     start=True, stop=True)
                last.then_inc(gate_done, 1)

        walk(pe, chains, blocks, do)



def ssm_attention_experts_kernel(nc, x, ssm, att, ffn, out):
    y_scratch = [nc.dram_tensor(f"y_scratch{k}", (2, 128, SEGS[k], CH, GE), F32).ap() for k in range(LAYERS)]
    hidden = nc.dram_tensor("hidden", (BATCH, TOKENS, E), F32).ap()
    attended = nc.dram_tensor("attended", (BATCH, TOKENS, E), F32).ap()
    spread = [nc.dram_tensor(f"spread{c}", (HALF, HEADS, SPREAD), F32).ap() for c in range(2)]
    with ExitStack() as ctx:
        state_space_layers(nc, ctx, x.rearrange("(n b) (q c) e -> n b q c e", b=2, c=TURNS), ssm, y_scratch,
                           hidden.rearrange("(n b) l e -> n b l e", b=2))
    with ExitStack() as ctx:
        attention(nc, ctx, att, hidden, spread, attended)
    with ExitStack() as ctx:
        experts(nc, ctx, ffn, attended.rearrange("(n b) l e -> n (b l) e", b=2),
                out.rearrange("(n b) l e -> n (b l) e", b=2))


def state_space_arrays(inputs):
    w_dbc, w_dt = inputs["L0_tok_W_dbc"], inputs["L0_tok_W_dt"]
    order = [feature_order(k) for k in range(LAYERS + 1)]
    pick = np.zeros((96, GE, 128), np.dtype("bfloat16"))
    for row in range(96):
        b, r = divmod(row % 32, GE)
        pick[row, r, E * b:E * (b + 1)] = 1
    halver = np.zeros((SEG, SEG // 2), np.float32)
    halver[np.arange(SEG), np.arange(SEG) // 2] = 0.5
    w_state = np.zeros((128, LAYERS, 2, 128), np.float32)
    w_delta = np.zeros((128, LAYERS, 128), np.float32)
    skip = np.zeros((128, LAYERS, 128), np.float32)
    for b in range(2):
        rows = slice(E * b, E * (b + 1))
        for k in range(LAYERS):
            for j in range(2):
                w_state[rows, k, j, rows] = w_dbc[k, 1 + E * j:1 + E * (j + 1)].T[order[k]]
            w_delta[rows, k, rows] = np.broadcast_to(w_dt[k, order[k], 0], (E, E))
            for j, f in enumerate(order[k + 1]):
                skip[E * b + order[k].index(f), k, E * b + j] = 1

    def twice(per_layer):
        return np.concatenate([np.stack(per_layer, 1)] * 2)

    return {"pick": pick, "ident": np.eye(128, dtype=np.float32), "halver": halver, "w_state": w_state,
            "w_dt": w_delta, "skip": skip,
            "rank_in": twice([w_dbc[k, 0, order[k]] for k in range(LAYERS)]),
            "b_dt": twice([inputs["L0_tok_b_dt"][k, order[k]] for k in range(LAYERS)]),
            "d_skip": twice([inputs["L0_tok_D"][k, order[k]] for k in range(LAYERS)]),
            "a_log": twice([inputs["L0_tok_A_log"][k, order[k]].T for k in range(LAYERS)])}


def attention_arrays(inputs):
    def get(name):
        return inputs["L0_attn_" + name]

    def with_rows(w, *rows):
        return np.concatenate([w.T] + [r.reshape(1, E) for r in rows])

    at = np.arange(REL, dtype=np.float32)[:, None]
    turns = at * np.exp(np.arange(0, E, 2, dtype=np.float32) * np.float32(-np.log(10000.0) / E))
    enc = np.stack([np.sin(turns), np.cos(turns)], axis=-1).reshape(REL, E).astype(np.float32)

    def heads_apart(w):
        out = np.zeros((w.shape[0], HEADS, ROWS), np.float32)
        out[:, :, 0:HEAD] = w.reshape(-1, HEADS, HEAD)
        return out.reshape(-1, HEADS * ROWS)

    w_q = np.stack([heads_apart(with_rows(get("Wq"), get("bq"), get(u + "_bias"))) for u in "uv"], 1)
    w_o = heads_apart(get("Wo")).T
    w_o[HEAD] = get("bo")
    return {"ident": np.eye(128, dtype=np.float32), "w_q": w_q,
            "w_k": heads_apart(with_rows(get("Wk"), get("bk"))), "w_v": heads_apart(with_rows(get("Wv"), get("bv"))),
            "w_o": w_o, "spare": np.eye(HEADS * ROWS, dtype=np.float32)[:, HEAD:HEAD + 1], "w_pos": heads_apart(with_rows(get("Wpos"), get("bpos"))),
            "enc": np.concatenate([enc.T, np.ones((1, REL), np.float32)]),
            "affine": np.stack([get("ln_gamma"), get("ln_beta")], 1)}


def expert_arrays(inputs):
    def get(name):
        return inputs["L0_ffn_" + name]

    w1 = get("w1").transpose(1, 0, 2).reshape(E, EXPERTS * HIDDEN)
    return {"ident": np.eye(128, dtype=np.float32), "w1": np.concatenate([w1, w1]), "b1": get("b1").T,
            "w2": get("w2").transpose(1, 0, 2), "b2": get("b2"), "gate": get("gate_w"),
            "gate_b": np.tile(get("gate_b"), (TILE, 1)),
            "ranks": np.tile(np.arange(EXPERTS, 0, -1, dtype=np.float32), (TILE, 1)),
            "gamma": np.tile(get("gamma"), (TILE, 1)), "beta": np.tile(get("beta"), (TILE, 1))}


def kernel(**inputs):
    import concourse.bacc as bacc
    from concourse.bass_utils import run_bass_kernel_spmd

    inputs = {name: np.asarray(a) for name, a in inputs.items()}
    nc = bacc.Bacc("TRN2", target_bir_lowering=False, num_devices=1)
    arrays = {}

    def place(name, a):
        a = np.ascontiguousarray(a)
        arrays[f"in_{name}_dram"] = a
        return nc.dram_tensor(f"in_{name}_dram", a.shape, mybir.dt.from_np(a.dtype), kind="ExternalInput").ap()

    x = place("x", inputs["x"])
    stages = [{name: place(f"{stage}_{name}", a) for name, a in of.items()}
              for stage, of in (("ssm", state_space_arrays(inputs)), ("att", attention_arrays(inputs)),
                                ("ffn", expert_arrays(inputs)))]
    out = nc.dram_tensor("out_0_dram", (BATCH, TOKENS, E), F32, kind="ExternalOutput").ap()
    ssm_attention_experts_kernel(nc, x, *stages, out)
    r = run_bass_kernel_spmd(nc, [arrays], core_ids=[0])
    return r.results[0]["out_0_dram"]
```
